# Optimizing a Trainium2 kernel written in Bass

```python
import numpy as np
import jax
import jax.numpy as jnp

def _softmax(x, axis=-1):
    return jax.nn.softmax(x, axis=axis)

def _gelu(x):
    return jax.nn.gelu(x, approximate=True)

def _silu(x):
    return jax.nn.silu(x)

def _sigmoid(x):
    return jax.nn.sigmoid(x)

def _layernorm(x, axis=-1, eps=1e-05):
    m = jnp.mean(x, axis=axis, keepdims=True)
    v = jnp.var(x, axis=axis, keepdims=True)
    return (x - m) / jnp.sqrt(v + eps)

def _scatter_add(tgt, idx, src, axis=0):
    return tgt.at[idx].add(src)

def _segment_sum(src, seg, n):
    return jax.ops.segment_sum(src, seg, n)
kernel_name = 'mk_adj_resnorm_d1_adj_r2_74f1f7'

def setup_inputs(seed: int=0):
    np.random.seed(seed)
    _w = jnp.asarray

    def _rec_inputs():
        import jax
        import jax.numpy as jnp
        _gk = jax.random.key(seed)
        x = -8.776e-05 + 1 * jax.random.normal(jax.random.fold_in(_gk, 1), (4096, 256), jnp.float32)
        _w = (1.0 + jnp.arange(4096, dtype=jnp.float32)) ** (-0.5)
        _w = _w / _w.mean()
        _pij = jnp.clip(0.00195312 * _w[:, None] * _w[None, :], 0.0, 1.0)
        _a = jax.random.uniform(jax.random.fold_in(_gk, 2), (4096, 4096)) < _pij
        _a = jnp.logical_or(_a, jnp.eye(4096, dtype=bool))
        _af = _a.astype(jnp.float32)
        _af = _af * jax.random.uniform(jax.random.fold_in(_gk, 3), (4096, 4096), jnp.float32, 0.05, 1)
        adj = _af
        return (x, adj)
    x, adj = _rec_inputs()

    def _L0_gnn_setup():
        import jax, jax.numpy as jnp
        import numpy as np
        N = 5000
        IN_F = 256
        OUT_F = 256
        key = jax.random.key(seed)
        k1, k2, k3 = jax.random.split(key, 3)
        x = jax.random.normal(k1, (N, IN_F), dtype=jnp.float32)
        adj = jax.random.uniform(k2, (N, N), dtype=jnp.float32)
        stdv = 1.0 / np.sqrt(OUT_F)
        weight = jax.random.uniform(k3, (IN_F, OUT_F), dtype=jnp.float32, minval=-stdv, maxval=stdv)
        t = jnp.ones((1,), dtype=jnp.float32)
        return {'x': x, 'adj': adj, 't': t, 'weight': weight}
    _L0_gnn_all = _L0_gnn_setup()
    _L0_gnn_in = {k: v for k, v in _L0_gnn_all.items() if k in ('t', 'weight')}
    del _L0_gnn_all
    return {'x': x, 'adj': adj, 'L0_gnn_t': _L0_gnn_in['t'], 'L0_gnn_weight': _L0_gnn_in['weight']}

def reference(x, adj, L0_gnn_t, L0_gnn_weight):
    import jax
    import jax.numpy as jnp

    def _L0_gnn_ref(x, adj, t, weight):
        import jax, jax.numpy as jnp
        import numpy as np
        N = 5000
        IN_F = 256
        OUT_F = 256
        ts = t[0]
        support = x @ weight
        return (1.0 - ts) * support + ts * (adj @ support)
    x = _layernorm(x + _L0_gnn_ref(x, adj, L0_gnn_t, L0_gnn_weight), axis=-1)
    return x

_drawn_inputs = setup_inputs


def setup_inputs(seed=0):
    import zlib

    import numpy as np

    out = dict(_drawn_inputs(seed))
    spreads = {}
    factors = {}
    for name, (base, spread) in spreads.items():
        noise = np.random.default_rng([zlib.crc32(name.encode()), seed]).standard_normal(out[name].shape)
        drawn = base * np.exp(spread * noise) if base else spread * noise
        out[name] = jnp.asarray(drawn.astype(out[name].dtype))
    for name, factor in factors.items():
        out[name] = (out[name] * factor).astype(out[name].dtype)
    return out
```

```python
from contextlib import ExitStack

import concourse.bass as bass
from concourse import mybir

F32 = mybir.dt.float32
F32R = mybir.dt.float32r
ALU = mybir.AluOpType
ACT = mybir.ActivationFunctionType

P = 128
N = 4096
C = 256
EPS = 1e-5

TILES = N // P
HALVES = C // P
ROW_TILES = 4
COLS = ROW_TILES * P
CHUNKS = TILES // ROW_TILES
PIECE = 2
PIECES = TILES // PIECE
RAW = 8
PARTS = 4
Z_AT = PARTS - 1
PROJECT_AT = 2
NORM_AT = PROJECT_AT + PARTS
STORE_AT = NORM_AT + 1
XT_AT = 10


def gnn_resnorm(nc: bass.Bass, x, xt, adjt, t, weight, out):
    ctx = ExitStack()
    with ctx:
        def sb(name, shape, dt=F32):
            return ctx.enter_context(nc.sbuf_tensor(name, shape, dt))

        def sem(name):
            return ctx.enter_context(nc.semaphore(name))

        x_raw = sb("x_raw", [P, TILES, C])
        x_hi = sb("x_hi", [P, TILES, C], F32R)
        x_lo = sb("x_lo", [P, TILES, C], F32R)
        adj_raw = sb("adj_raw", [P, RAW, PIECE * COLS])
        adj_hi = sb("adj_hi", [P, PARTS, PIECE * COLS], F32R)
        adj_lo = sb("adj_lo", [P, PARTS, PIECE * COLS], F32R)
        xt_sb = sb("xt_sb", [P, 2, HALVES, COLS])
        z = sb("z", [P, HALVES, COLS])
        z_hi = sb("z_hi", [P, HALVES, COLS], F32R)
        z_lo = sb("z_lo", [P, HALVES, COLS], F32R)
        w_raw = sb("w_raw", [P, HALVES * C])
        w_hi = sb("w_hi", [P, HALVES * C], F32R)
        w_lo = sb("w_lo", [P, HALVES * C], F32R)
        t_col = sb("t_col", [P, 1])
        one_minus_t = sb("one_minus_t", [P, 1])
        summed = sb("summed", [P, ROW_TILES, C])
        normed = sb("normed", [P, 2, ROW_TILES * C])
        stats = sb("stats", [P, ROW_TILES, 6])
        mean_sum = sb("mean_sum", [P, ROW_TILES])
        mean_diff = sb("mean_diff", [P, ROW_TILES])
        squares = sb("squares", [P, ROW_TILES])
        between = sb("between", [P, ROW_TILES])
        var_eps = sb("var_eps", [P, ROW_TILES])
        std = sb("std", [P, ROW_TILES])
        rough = sb("rough", [P, ROW_TILES])
        half_vr = sb("half_vr", [P, ROW_TILES])
        half_vrr = sb("half_vrr", [P, ROW_TILES])
        rstd = sb("rstd", [P, ROW_TILES])
        shift = sb("shift", [P, ROW_TILES])

        y_ps = [[ctx.enter_context(nc.psum_tensor(f"y_ps{b}{h}", [P, COLS], F32)) for h in range(HALVES)]
                for b in range(2)]
        proj_ps = [ctx.enter_context(nc.psum_tensor(f"proj_ps{r}", [P, COLS], F32)) for r in range(ROW_TILES)]

        adj_landed = [sem(f"adj_landed{s}") for s in range(RAW)]
        x_landed = [sem(f"x_landed{k}") for k in range(PIECES)]
        xt_landed = [sem(f"xt_landed{b}") for b in range(2)]
        w_landed = sem("w_landed")
        t_landed = sem("t_landed")
        x_hi_made = sem("x_hi_made")
        x_lo_made = sem("x_lo_made")
        w_hi_made = sem("w_hi_made")
        w_lo_made = sem("w_lo_made")
        t_made = sem("t_made")
        adj_hi_made = sem("adj_hi_made")
        adj_lo_made = sem("adj_lo_made")
        adj_used = sem("adj_used")
        xt_scaled = sem("xt_scaled")
        z_made = sem("z_made")
        z_hi_made = sem("z_hi_made")
        z_lo_made = sem("z_lo_made")
        projected = sem("projected")
        sum_made = sem("sum_made")
        stats_made = sem("stats_made")
        moments_made = sem("moments_made")
        between_made = sem("between_made")
        var_made = sem("var_made")
        std_made = sem("std_made")
        rough_made = sem("rough_made")
        half_vr_made = sem("half_vr_made")
        half_vrr_made = sem("half_vrr_made")
        rstd_made = sem("rstd_made")
        shift_made = sem("shift_made")
        norm_made = sem("norm_made")
        stored = [sem(f"stored{b}") for b in range(2)]

        out_v = out.rearrange("(p i) f -> p (i f)", i=TILES)

        def chunks(eng, body):
            body(0, 0)
            with eng.Fori(1, CHUNKS - 1, 2) as q:
                body(q, 1)
                body(q + 1, 0)
            body(CHUNKS - 1, 1)

        def static(q):
            return isinstance(q, int)

        block = ctx.enter_context(nc.Block())

        @block.sync
        def _(sp):
            sp.dma_start(t_col[:, :], t.rearrange("(a b) -> a b", a=1).broadcast_to((P, 1))).then_inc(t_landed, 16)

            def load(q, b):
                for k in range(PIECES):
                    if static(q) and q == 0:
                        sp.dma_start(x_raw[:, k * PIECE:(k + 1) * PIECE, :],
                                     x[:, k * PIECE * C:(k + 1) * PIECE * C]).then_inc(x_landed[k], 16)
                    if not static(q) or q > 0 or k >= RAW:
                        sp.wait_ge(adj_lo_made, q * PIECES + (k + 1 - RAW))
                    sp.dma_start(adj_raw[:, k % RAW, :],
                                 adjt[bass.ds(q, 1), :, k * PIECE * COLS:(k + 1) * PIECE * COLS]
                                 .rearrange("a p n -> (a p) n")).then_inc(adj_landed[k % RAW], 16)
                    if k == RAW - 1:
                        if not static(q) or q > 1:
                            sp.wait_ge(z_made, HALVES * (q - 1))
                        sp.dma_start(xt_sb[:, b, :, :], xt[bass.ds(q, 1), :, :, :]
                                     .rearrange("a p h n -> (a p) h n")).then_inc(xt_landed[b], 16)
                        if static(q) and q == 0:
                            sp.dma_start(w_raw[:, :].rearrange("p (h f) -> p h f", h=HALVES),
                                         weight.rearrange("(h p) f -> p h f", p=P)).then_inc(w_landed, 16)

            chunks(sp, load)

        @block.scalar
        def _(act):
            def z_high(q):
                for h in range(HALVES):
                    act.wait_ge(z_made, q * HALVES + (h + 1))
                    if h == 0 and (not static(q) or q > 0):
                        act.wait_ge(projected, q * ROW_TILES)
                    nc.scalar.activation(z_hi[:, h, :], z[:, h, :], ACT.Copy).then_inc(z_hi_made, 1)

            def root(q):
                act.wait_ge(var_made, q + 1)
                nc.scalar.activation(std[:, :], var_eps[:, :], ACT.Sqrt).then_inc(std_made, 1)

            def finish(q, b):
                act.wait_ge(shift_made, q + 1)
                if not static(q) or q > 1:
                    act.wait_ge(stored[b], store_count(q, b) - 16)
                for r in range(ROW_TILES):
                    nc.scalar.activation(normed[:, b, r * C:(r + 1) * C], summed[:, r, :], ACT.Identity,
                                         bias=shift[:, r:r + 1], scale=rstd[:, r:r + 1]).then_inc(norm_made, 1)
                act.wait_ge(norm_made, (q + 1) * ROW_TILES)
                act.dma_start(out_v[:, bass.ds(q * (ROW_TILES * C), ROW_TILES * C)],
                              normed[:, b, :]).then_inc(stored[b], 16)

            def store_count(q, b):
                return (q - b) * 8 + 16

            def split(q, b):
                for k in range(PIECES):
                    if static(q) and q == 0:
                        act.wait_ge(x_landed[k], 16)
                        nc.scalar.activation(x_hi[:, k * PIECE:(k + 1) * PIECE, :],
                                             x_raw[:, k * PIECE:(k + 1) * PIECE, :], ACT.Copy).then_inc(x_hi_made, 1)
                    act.wait_ge(adj_landed[k % RAW], q * (16 * PIECES // RAW) + 16 * (k // RAW + 1))
                    if not static(q) or q > 0 or k >= PARTS:
                        act.wait_ge(adj_used, q * PIECES + (k + 1 - PARTS))
                    nc.scalar.activation(adj_hi[:, k % PARTS, :], adj_raw[:, k % RAW, :],
                                         ACT.Copy).then_inc(adj_hi_made, 1)
                    if static(q) and q == 0:
                        if k == XT_AT:
                            act.wait_ge(w_landed, 16)
                            nc.scalar.activation(w_hi[:, :], w_raw[:, :], ACT.Copy).then_inc(w_hi_made, 1)
                        continue
                    if k == Z_AT:
                        z_high(q - 1)
                    if k == NORM_AT:
                        root(q - 1)
                    if k == STORE_AT:
                        finish(q - 1, 1 - b)

            chunks(act, split)
            z_high(CHUNKS - 1)
            root(CHUNKS - 1)
            finish(CHUNKS - 1, 1)
            for b in range(2):
                act.wait_ge(stored[b], store_count(CHUNKS - 2 + b, b))

        @block.vector
        def _(dve):
            def scale_xt(q, b):
                dve.wait_ge(xt_landed[b], (q - b) * 8 + 16)
                nc.vector.tensor_scalar(xt_sb[:, b, :, :], xt_sb[:, b, :, :], one_minus_t[:, 0:1], None,
                                        ALU.mult).then_inc(xt_scaled, 1)

            def make_z(q, b):
                dve.wait_ge(adj_used, (q + 1) * PIECES)
                dve.wait_ge(xt_scaled, q + 1)
                for h in range(HALVES):
                    if h == 0 and (not static(q) or q > 0):
                        dve.wait_ge(z_hi_made, q * HALVES)
                        dve.wait_ge(z_lo_made, q * HALVES)
                    nc.vector.scalar_tensor_tensor(out=z[:, h, :], in0=y_ps[b][h][:, :], scalar=t_col[:, 0:1],
                                                   in1=xt_sb[:, b, h, :], op0=ALU.mult,
                                                   op1=ALU.add).then_inc(z_made, 1)
                for h in range(HALVES):
                    dve.wait_ge(z_hi_made, q * HALVES + (h + 1))
                    nc.vector.tensor_tensor(z_lo[:, h, :], z[:, h, :], z_hi[:, h, :].bitcast(F32),
                                            ALU.subtract).then_inc(z_lo_made, 1)

            def layernorm(q, b):
                if not static(q) or q > 0:
                    dve.wait_ge(norm_made, q * ROW_TILES)
                for r in range(ROW_TILES):
                    dve.wait_ge(projected, q * ROW_TILES + (r + 1))
                    nc.vector.tensor_tensor(summed[:, r, :], proj_ps[r][:, 0:C],
                                            x_raw[:, bass.ds(q * ROW_TILES + r, 1), :]
                                            .rearrange("p a f -> p (a f)"), ALU.add).then_inc(sum_made, 1)
                for r in range(ROW_TILES):
                    dve.wait_ge(sum_made, q * ROW_TILES + (r + 1))
                    nc.vector.bn_stats(stats[:, r, :], summed[:, r, :]).then_inc(stats_made, 1)
                dve.wait_ge(stats_made, (q + 1) * ROW_TILES)
                nc.vector.tensor_tensor(mean_sum[:, :], stats[:, :, 1], stats[:, :, 4], ALU.add).then_inc(moments_made, 1)
                nc.vector.tensor_tensor(mean_diff[:, :], stats[:, :, 1], stats[:, :, 4],
                                        ALU.subtract).then_inc(moments_made, 1)
                nc.vector.scalar_tensor_tensor(out=squares[:, :], in0=stats[:, :, 2], scalar=C * EPS,
                                               in1=stats[:, :, 5], op0=ALU.add, op1=ALU.add).then_inc(moments_made, 1)
                dve.wait_ge(moments_made, (q + 1) * 3)
                nc.vector.scalar_tensor_tensor(out=between[:, :], in0=mean_diff[:, :], scalar=0.25,
                                               in1=mean_diff[:, :], op0=ALU.mult, op1=ALU.mult).then_inc(between_made, 1)
                dve.wait_ge(between_made, q + 1)
                nc.vector.scalar_tensor_tensor(out=var_eps[:, :], in0=squares[:, :], scalar=1.0 / C,
                                               in1=between[:, :], op0=ALU.mult, op1=ALU.add).then_inc(var_made, 1)
                dve.wait_ge(std_made, q + 1)
                nc.vector.reciprocal(rough[:, :], std[:, :]).then_inc(rough_made, 1)
                dve.wait_ge(rough_made, q + 1)
                nc.vector.scalar_tensor_tensor(out=half_vr[:, :], in0=var_eps[:, :], scalar=-0.5,
                                               in1=rough[:, :], op0=ALU.mult, op1=ALU.mult).then_inc(half_vr_made, 1)
                dve.wait_ge(half_vr_made, q + 1)
                nc.vector.tensor_tensor(half_vrr[:, :], half_vr[:, :], rough[:, :],
                                        ALU.mult).then_inc(half_vrr_made, 1)
                dve.wait_ge(half_vrr_made, q + 1)
                nc.vector.scalar_tensor_tensor(out=rstd[:, :], in0=half_vrr[:, :], scalar=1.5,
                                               in1=rough[:, :], op0=ALU.add, op1=ALU.mult).then_inc(rstd_made, 1)
                dve.wait_ge(rstd_made, q + 1)
                nc.vector.scalar_tensor_tensor(out=shift[:, :], in0=mean_sum[:, :], scalar=-0.5,
                                               in1=rstd[:, :], op0=ALU.mult, op1=ALU.mult).then_inc(shift_made, 1)

            def split(q, b):
                for k in range(PIECES):
                    if static(q) and q == 0:
                        dve.wait_ge(x_hi_made, k + 1)
                        nc.vector.tensor_tensor(x_lo[:, k * PIECE:(k + 1) * PIECE, :],
                                                x_raw[:, k * PIECE:(k + 1) * PIECE, :],
                                                x_hi[:, k * PIECE:(k + 1) * PIECE, :].bitcast(F32),
                                                ALU.subtract).then_inc(x_lo_made, 1)
                    dve.wait_ge(adj_hi_made, q * PIECES + (k + 1))
                    nc.vector.tensor_tensor(adj_lo[:, k % PARTS, :], adj_raw[:, k % RAW, :],
                                            adj_hi[:, k % PARTS, :].bitcast(F32),
                                            ALU.subtract).then_inc(adj_lo_made, 1)
                    if k == XT_AT:
                        if static(q) and q == 0:
                            dve.wait_ge(w_hi_made, 1)
                            nc.vector.tensor_tensor(w_lo[:, :], w_raw[:, :], w_hi[:, :].bitcast(F32),
                                                    ALU.subtract).then_inc(w_lo_made, 1)
                        scale_xt(q, b)
                    if static(q) and q == 0:
                        continue
                    if k == Z_AT:
                        make_z(q - 1, 1 - b)
                    if k == NORM_AT:
                        layernorm(q - 1, 1 - b)

            dve.wait_ge(t_landed, 16)
            nc.vector.tensor_scalar(one_minus_t[:, :], t_col[:, :], -1.0, 1.0, ALU.mult, ALU.add).then_inc(t_made, 1)
            dve.wait_ge(t_made, 1)
            chunks(dve, split)
            make_z(CHUNKS - 1, 1)
            layernorm(CHUNKS - 1, 1)

        @block.tensor
        def _(pe):
            def project(q):
                if static(q) and q == 0:
                    pe.wait_ge(w_lo_made, 1)
                pe.wait_ge(z_hi_made, (q + 1) * HALVES)
                pe.wait_ge(z_lo_made, (q + 1) * HALVES)
                if not static(q) or q > 0:
                    pe.wait_ge(sum_made, q * ROW_TILES)
                for r in range(ROW_TILES):
                    rows = slice(r * P, (r + 1) * P)
                    for h in range(HALVES):
                        feats = slice(h * C, (h + 1) * C)
                        for i, (zp, wp) in enumerate([(z_hi, w_hi), (z_hi, w_lo), (z_lo, w_hi)]):
                            last = nc.tensor.matmul(proj_ps[r][:, 0:C], zp[:, h, rows], wp[:, feats],
                                                    start=(h == 0 and i == 0), stop=(h == HALVES - 1 and i == 2))
                    last.then_inc(projected, 1)

            def aggregate(q, b):
                if not static(q) or q > 1:
                    pe.wait_ge(z_made, (q - 1) * HALVES)
                for k in range(PIECES):
                    if static(q) and q == 0:
                        pe.wait_ge(x_lo_made, k + 1)
                    pe.wait_ge(adj_lo_made, q * PIECES + (k + 1))
                    for j in range(PIECE):
                        tile = k * PIECE + j
                        cols = slice(j * COLS, (j + 1) * COLS)
                        for h in range(HALVES):
                            feats = slice(h * P, (h + 1) * P)
                            for i, (xp, ap) in enumerate([(x_hi, adj_hi), (x_hi, adj_lo), (x_lo, adj_hi)]):
                                last = nc.tensor.matmul(y_ps[b][h][:, :], xp[:, tile, feats], ap[:, k % PARTS, cols],
                                                        start=(tile == 0 and i == 0),
                                                        stop=(tile == TILES - 1 and i == 2))
                    last.then_inc(adj_used, 1)
                    if k == PROJECT_AT and (not static(q) or q > 0):
                        project(q - 1)

            chunks(pe, aggregate)
            project(CHUNKS - 1)


def kernel(x, adj, L0_gnn_t, L0_gnn_weight):
    import numpy as _np
    import concourse.bacc as _bacc
    from concourse import mybir as _mybir
    from concourse.bass_utils import run_bass_kernel_spmd as _run

    x, adj = _np.asarray(x), _np.asarray(adj)
    arrays = {
        "x_rows": x.reshape(P, TILES * C),
        "x_cols": x.reshape(P, CHUNKS, ROW_TILES, HALVES, P).transpose(1, 4, 3, 2, 0)
                   .reshape(CHUNKS, P, HALVES, COLS),
        "adj_cols": adj.reshape(P, CHUNKS, ROW_TILES, P, TILES).transpose(1, 3, 4, 2, 0)
                       .reshape(CHUNKS, P, TILES * COLS),
        "t": _np.asarray(L0_gnn_t),
        "weight": _np.asarray(L0_gnn_weight),
    }
    arrays = {name: _np.ascontiguousarray(a) for name, a in arrays.items()}
    nc = _bacc.Bacc("TRN2", target_bir_lowering=False, num_devices=1)
    args = [nc.dram_tensor(name, a.shape, _mybir.dt.from_np(a.dtype), kind="ExternalInput").ap()
            for name, a in arrays.items()]
    args.append(nc.dram_tensor("out", (N, C), F32, kind="ExternalOutput").ap())
    gnn_resnorm(nc, *args)
    r = _run(nc, [arrays], core_ids=[0])
    return r.results[0]["out"]
```

```python
from contextlib import ExitStack

import concourse.bass as bass
from concourse import mybir

F32 = mybir.dt.float32
F32R = mybir.dt.float32r
ALU = mybir.AluOpType
ACT = mybir.ActivationFunctionType

P = 128
N = 4096
C = 256
EPS = 1e-5

TILES = N // P
HALVES = C // P
ROW_TILES = 4
COLS = ROW_TILES * P
CHUNKS = TILES // ROW_TILES
PIECE = 2
PIECES = TILES // PIECE
RAW = 8
PARTS = 4
Z_AT = PARTS - 1
PROJECT_AT = 2
NORM_AT = PROJECT_AT + PARTS
STORE_AT = NORM_AT + 1
STORED_AT = STORE_AT + PARTS
XT_AT = 10
ROWS_A, ROWS_B = slice(0, COLS // 2), slice(COLS // 2, COLS)
WARM = 7


def gnn_resnorm(nc: bass.Bass, x, xt, adjt, t, weight, out):
    ctx = ExitStack()
    with ctx:
        def sb(name, shape, dt=F32):
            return ctx.enter_context(nc.sbuf_tensor(name, shape, dt))

        def sem(name):
            return ctx.enter_context(nc.semaphore(name))

        x_raw = sb("x_raw", [P, TILES, C])
        x_hi = sb("x_hi", [P, TILES, C], F32R)
        x_lo = sb("x_lo", [P, TILES, C], F32R)
        adj_raw = sb("adj_raw", [P, RAW, PIECE * COLS])
        adj_hi = sb("adj_hi", [P, PARTS, PIECE * COLS], F32R)
        adj_lo = sb("adj_lo", [P, PARTS, PIECE * COLS], F32R)
        xt_sb = sb("xt_sb", [P, 2, HALVES, COLS])
        z = sb("z", [P, HALVES, COLS])
        z_hi = sb("z_hi", [P, HALVES, COLS], F32R)
        z_lo = sb("z_lo", [P, HALVES, COLS], F32R)
        w_raw = sb("w_raw", [P, HALVES * C])
        w_hi = sb("w_hi", [P, HALVES * C], F32R)
        w_lo = sb("w_lo", [P, HALVES * C], F32R)
        idle = sb("idle", [P, COLS], mybir.dt.bfloat16)
        t_col = sb("t_col", [P, 1])
        one_minus_t = sb("one_minus_t", [P, 1])
        summed = sb("summed", [P, ROW_TILES, C])
        normed = sb("normed", [P, ROW_TILES * C])
        stats = sb("stats", [P, ROW_TILES, 6])
        mean_sum = sb("mean_sum", [P, ROW_TILES])
        mean_diff = sb("mean_diff", [P, ROW_TILES])
        squares = sb("squares", [P, ROW_TILES])
        between = sb("between", [P, ROW_TILES])
        var_eps = sb("var_eps", [P, ROW_TILES])
        std = sb("std", [P, ROW_TILES])
        rough = sb("rough", [P, ROW_TILES])
        half_vr = sb("half_vr", [P, ROW_TILES])
        half_vrr = sb("half_vrr", [P, ROW_TILES])
        rstd = sb("rstd", [P, ROW_TILES])
        shift = sb("shift", [P, ROW_TILES])

        y_ps = [ctx.enter_context(nc.psum_tensor(f"y_ps{b}", [P, HALVES, COLS], F32)) for b in range(2)]
        proj_ps = [ctx.enter_context(nc.psum_tensor(f"proj_ps{r}", [P, COLS], F32)) for r in range(ROW_TILES)]

        adj_landed = [sem(f"adj_landed{s}") for s in range(RAW)]
        x_landed = [sem(f"x_landed{k}") for k in range(PIECES)]
        xt_landed = [sem(f"xt_landed{b}") for b in range(2)]
        w_landed = sem("w_landed")
        t_landed = sem("t_landed")
        idle_made = sem("idle_made")
        first_adj_landed = sem("first_adj_landed")
        first_x_landed = sem("first_x_landed")
        first_x_hi_made = sem("first_x_hi_made")
        first_x_lo_made = sem("first_x_lo_made")
        first_adj_hi_made = sem("first_adj_hi_made")
        first_adj_lo_made = sem("first_adj_lo_made")
        x_hi_made = sem("x_hi_made")
        x_lo_made = sem("x_lo_made")
        w_hi_made = sem("w_hi_made")
        w_lo_made = sem("w_lo_made")
        t_made = sem("t_made")
        adj_hi_made = sem("adj_hi_made")
        adj_lo_made = sem("adj_lo_made")
        adj_used = sem("adj_used")
        xt_scaled = sem("xt_scaled")
        z_made = sem("z_made")
        last_y_made = sem("last_y_made")
        last_z_made = sem("last_z_made")
        z_hi_made = sem("z_hi_made")
        z_lo_made = sem("z_lo_made")
        projected = sem("projected")
        sum_made = sem("sum_made")
        stats_made = sem("stats_made")
        moments_made = sem("moments_made")
        between_made = sem("between_made")
        var_made = sem("var_made")
        std_made = sem("std_made")
        rough_made = sem("rough_made")
        half_vr_made = sem("half_vr_made")
        half_vrr_made = sem("half_vrr_made")
        rstd_made = sem("rstd_made")
        shift_made = sem("shift_made")
        norm_made = sem("norm_made")
        stored = sem("stored")
        last_norm_made = sem("last_norm_made")
        last_stored = [sem(f"last_stored{n}") for n in range(2)]

        out_v = out.rearrange("(p i) f -> p (i f)", i=TILES)

        def chunks(eng, body):
            body(0, 0)
            with nc.Fori(1, CHUNKS - 1, 2, engines=[eng.engine], hint_back_edge=True) as q:
                body(q, 1)
                body(q + 1, 0)
            body(CHUNKS - 1, 1)

        def static(q):
            return isinstance(q, int)

        block = ctx.enter_context(nc.Block())

        @block.sync
        def _(sp):
            sp.dma_start(adj_raw[:, 0, 0:COLS], adjt[0, 0, :, 0:COLS]).then_inc(first_adj_landed, 16)

            def load(q, b):
                for k in range(PIECES):
                    if static(q) and q == 0 and k == 0:
                        sp.dma_start(x_raw[:, 1:PIECE, :], x[:, C:PIECE * C]).then_inc(x_landed[0], 16)
                        sp.dma_start(adj_raw[:, 0, COLS:PIECE * COLS],
                                     adjt[0, 0, :, COLS:PIECE * COLS]).then_inc(adj_landed[0], 16)
                        continue
                    if static(q) and q == 0:
                        sp.dma_start(x_raw[:, k * PIECE:(k + 1) * PIECE, :],
                                     x[:, k * PIECE * C:(k + 1) * PIECE * C]).then_inc(x_landed[k], 16)
                    if not static(q) or q > 0 or k >= RAW:
                        sp.wait_ge(adj_lo_made, q * PIECES + (k + 1 - RAW))
                    sp.dma_start(adj_raw[:, k % RAW, :],
                                 adjt[bass.ds(q, 1), k, :, :]
                                 .rearrange("a p n -> (a p) n")).then_inc(adj_landed[k % RAW], 16)
                    if k == RAW - 1:
                        sp.dma_start(xt_sb[:, b, :, :], xt[bass.ds(q, 1), :, :, :]
                                     .rearrange("a p h n -> (a p) h n")).then_inc(xt_landed[b], 16)
                        if static(q) and q == 0:
                            sp.dma_start(t_col[:, :], t.rearrange("(a b) -> a b", a=1)
                                         .broadcast_to((P, 1))).then_inc(t_landed, 16)
                            sp.dma_start(w_raw[:, :].rearrange("p (h f) -> p h f", h=HALVES),
                                         weight.rearrange("(h p) f -> p h f", p=P)).then_inc(w_landed, 16)

            chunks(sp, load)

        @block.scalar
        def _(act):
            def z_high(q):
                for h in range(HALVES):
                    act.wait_ge(z_made, q * HALVES + (h + 1))
                    nc.scalar.activation(z_hi[:, h, :], z[:, h, :], ACT.Copy).then_inc(z_hi_made, 1)

            def root(n, rows=slice(0, ROW_TILES)):
                act.wait_ge(var_made, n + 1)
                nc.scalar.activation(std[:, rows], var_eps[:, rows], ACT.Sqrt).then_inc(std_made, 1)

            def finish(q):
                act.wait_ge(shift_made, q + 1)
                for r in range(ROW_TILES):
                    nc.scalar.activation(normed[:, r * C:(r + 1) * C], summed[:, r, :], ACT.Identity,
                                         bias=shift[:, r:r + 1], scale=rstd[:, r:r + 1]).then_inc(norm_made, 1)
                act.wait_ge(norm_made, (q + 1) * ROW_TILES)
                act.dma_start(out_v[:, bass.ds(q * (ROW_TILES * C), ROW_TILES * C)],
                              normed[:, :]).then_inc(stored, 16)

            def split(q, b):
                for k in range(PIECES):
                    lead = 1 if static(q) and q == 0 and k == 0 else 0
                    if static(q) and q == 0:
                        tiles = slice(k * PIECE + lead, (k + 1) * PIECE)
                        act.wait_ge(x_landed[k], 16)
                        nc.scalar.activation(x_hi[:, tiles, :], x_raw[:, tiles, :], ACT.Copy).then_inc(x_hi_made, 1)
                    act.wait_ge(adj_landed[k % RAW], q * (16 * PIECES // RAW) + 16 * (k // RAW + 1))
                    if not static(q) or q > 0 or k >= PARTS:
                        act.wait_ge(adj_used, q * PIECES + (k + 1 - PARTS))
                    nc.scalar.activation(adj_hi[:, k % PARTS, lead * COLS:], adj_raw[:, k % RAW, lead * COLS:],
                                         ACT.Copy).then_inc(adj_hi_made, 1)
                    if static(q) and q == 0:
                        if k == XT_AT:
                            act.wait_ge(w_landed, 16)
                            nc.scalar.activation(w_hi[:, :], w_raw[:, :], ACT.Copy).then_inc(w_hi_made, 1)
                        continue
                    if k == Z_AT:
                        z_high(q - 1)
                    if k == NORM_AT:
                        root(q - 1)
                    if k == STORE_AT:
                        finish(q - 1)
                    if k == STORED_AT:
                        act.wait_ge(stored, q * 16)

            act.dma_start(x_raw[:, 0, :], x[:, 0:C]).then_inc(first_x_landed, 16)
            act.wait_ge(first_adj_landed, 16)
            nc.scalar.activation(adj_hi[:, 0, 0:COLS], adj_raw[:, 0, 0:COLS], ACT.Copy).then_inc(first_adj_hi_made, 1)
            chunks(act, split)

            for n in range(2):
                root(CHUNKS - 1 + n, slice(2 * n, 2 * n + 2))
                act.wait_ge(shift_made, CHUNKS + n)
                r = 2 * n + 1
                nc.scalar.activation(normed[:, r * C:(r + 1) * C], summed[:, r, :], ACT.Identity,
                                     bias=shift[:, r:r + 1], scale=rstd[:, r:r + 1]).then_inc(norm_made, 1)
                act.wait_ge(norm_made, (CHUNKS - 1) * ROW_TILES + n + 1)
                act.wait_ge(last_norm_made, n + 1)
                act.dma_start(out_v[:, (TILES - 4 + 2 * n) * C:(TILES - 2 + 2 * n) * C],
                              normed[:, 2 * n * C:(2 * n + 2) * C]).then_inc(last_stored[n], 16)
            for n in range(2):
                act.wait_ge(last_stored[n], 16)

        @block.vector
        def _(dve):
            def scale_xt(q, b):
                dve.wait_ge(xt_landed[b], (q - b) * 8 + 16)
                nc.vector.tensor_scalar(xt_sb[:, b, :, :], xt_sb[:, b, :, :], one_minus_t[:, 0:1], None,
                                        ALU.mult).then_inc(xt_scaled, 1)

            def make_z(q, b):
                dve.wait_ge(adj_used, (q + 1) * PIECES)
                dve.wait_ge(xt_scaled, q + 1)
                for h in range(HALVES):
                    nc.vector.scalar_tensor_tensor(out=z[:, h, :], in0=y_ps[b][:, h, :], scalar=t_col[:, 0:1],
                                                   in1=xt_sb[:, b, h, :], op0=ALU.mult,
                                                   op1=ALU.add).then_inc(z_made, 1)
                for h in range(HALVES):
                    dve.wait_ge(z_hi_made, q * HALVES + (h + 1))
                    nc.vector.tensor_tensor(z_lo[:, h, :], z[:, h, :], z_hi[:, h, :].bitcast(F32),
                                            ALU.subtract).then_inc(z_lo_made, 1)

            def sums(q, rows=slice(0, ROW_TILES)):
                for r in range(rows.start, rows.stop):
                    dve.wait_ge(projected, q * ROW_TILES + (r + 1))
                    nc.vector.tensor_tensor(summed[:, r, :], proj_ps[r][:, 0:C],
                                            x_raw[:, bass.ds(q * ROW_TILES + r, 1), :]
                                            .rearrange("p a f -> p (a f)"), ALU.add).then_inc(sum_made, 1)
                for r in range(rows.start, rows.stop):
                    dve.wait_ge(sum_made, q * ROW_TILES + (r + 1))
                    nc.vector.bn_stats(stats[:, r, :], summed[:, r, :]).then_inc(stats_made, 1)

            def scale_and_shift(q, n, rows=slice(0, ROW_TILES)):
                dve.wait_ge(stats_made, q * ROW_TILES + rows.stop)
                nc.vector.tensor_tensor(mean_sum[:, rows], stats[:, rows, 1], stats[:, rows, 4],
                                        ALU.add).then_inc(moments_made, 1)
                nc.vector.tensor_tensor(mean_diff[:, rows], stats[:, rows, 1], stats[:, rows, 4],
                                        ALU.subtract).then_inc(moments_made, 1)
                nc.vector.scalar_tensor_tensor(out=squares[:, rows], in0=stats[:, rows, 2], scalar=C * EPS,
                                               in1=stats[:, rows, 5], op0=ALU.add, op1=ALU.add).then_inc(moments_made, 1)
                dve.wait_ge(moments_made, (n + 1) * 3)
                nc.vector.scalar_tensor_tensor(out=between[:, rows], in0=mean_diff[:, rows], scalar=0.25,
                                               in1=mean_diff[:, rows], op0=ALU.mult, op1=ALU.mult).then_inc(between_made, 1)
                dve.wait_ge(between_made, n + 1)
                nc.vector.scalar_tensor_tensor(out=var_eps[:, rows], in0=squares[:, rows], scalar=1.0 / C,
                                               in1=between[:, rows], op0=ALU.mult, op1=ALU.add).then_inc(var_made, 1)
                dve.wait_ge(std_made, n + 1)
                nc.vector.reciprocal(rough[:, rows], std[:, rows]).then_inc(rough_made, 1)
                dve.wait_ge(rough_made, n + 1)
                nc.vector.scalar_tensor_tensor(out=half_vr[:, rows], in0=var_eps[:, rows], scalar=-0.5,
                                               in1=rough[:, rows], op0=ALU.mult, op1=ALU.mult).then_inc(half_vr_made, 1)
                dve.wait_ge(half_vr_made, n + 1)
                nc.vector.tensor_tensor(half_vrr[:, rows], half_vr[:, rows], rough[:, rows],
                                        ALU.mult).then_inc(half_vrr_made, 1)
                dve.wait_ge(half_vrr_made, n + 1)
                nc.vector.scalar_tensor_tensor(out=rstd[:, rows], in0=half_vrr[:, rows], scalar=1.5,
                                               in1=rough[:, rows], op0=ALU.add, op1=ALU.mult).then_inc(rstd_made, 1)
                dve.wait_ge(rstd_made, n + 1)
                nc.vector.scalar_tensor_tensor(out=shift[:, rows], in0=mean_sum[:, rows], scalar=-0.5,
                                               in1=rstd[:, rows], op0=ALU.mult, op1=ALU.mult).then_inc(shift_made, 1)

            def split(q, b):
                for k in range(PIECES):
                    lead = 1 if static(q) and q == 0 and k == 0 else 0
                    if static(q) and q == 0:
                        tiles = slice(k * PIECE + lead, (k + 1) * PIECE)
                        dve.wait_ge(x_hi_made, k + 1)
                        nc.vector.tensor_tensor(x_lo[:, tiles, :], x_raw[:, tiles, :], x_hi[:, tiles, :].bitcast(F32),
                                                ALU.subtract).then_inc(x_lo_made, 1)
                    dve.wait_ge(adj_hi_made, q * PIECES + (k + 1))
                    nc.vector.tensor_tensor(adj_lo[:, k % PARTS, lead * COLS:], adj_raw[:, k % RAW, lead * COLS:],
                                            adj_hi[:, k % PARTS, lead * COLS:].bitcast(F32),
                                            ALU.subtract).then_inc(adj_lo_made, 1)
                    if k == XT_AT:
                        if static(q) and q == 0:
                            dve.wait_ge(t_landed, 16)
                            nc.vector.tensor_scalar(one_minus_t[:, :], t_col[:, :], -1.0, 1.0, ALU.mult,
                                                    ALU.add).then_inc(t_made, 1)
                            dve.wait_ge(t_made, 1)
                            dve.wait_ge(w_hi_made, 1)
                            nc.vector.tensor_tensor(w_lo[:, :], w_raw[:, :], w_hi[:, :].bitcast(F32),
                                                    ALU.subtract).then_inc(w_lo_made, 1)
                        scale_xt(q, b)
                    if static(q) and q == 0:
                        continue
                    if k == Z_AT:
                        make_z(q - 1, 1 - b)
                    if k == NORM_AT:
                        sums(q - 1)
                        scale_and_shift(q - 1, q - 1)

            nc.vector.memset(idle[:, :], 0.0).then_inc(idle_made, 1)
            dve.wait_ge(first_x_landed, 16)
            nc.vector.tensor_copy(x_hi[:, 0, :], x_raw[:, 0, :]).then_inc(first_x_hi_made, 1)
            dve.wait_ge(first_x_hi_made, 1)
            nc.vector.tensor_tensor(x_lo[:, 0, :], x_raw[:, 0, :], x_hi[:, 0, :].bitcast(F32),
                                    ALU.subtract).then_inc(first_x_lo_made, 1)
            dve.wait_ge(first_adj_hi_made, 1)
            nc.vector.tensor_tensor(adj_lo[:, 0, 0:COLS], adj_raw[:, 0, 0:COLS], adj_hi[:, 0, 0:COLS].bitcast(F32),
                                    ALU.subtract).then_inc(first_adj_lo_made, 1)
            chunks(dve, split)

            def last_z(cols, halves, b, n):
                dve.wait_ge(last_y_made, n)
                nc.vector.scalar_tensor_tensor(out=z[:, halves, cols], in0=y_ps[b][:, halves, cols],
                                               scalar=t_col[:, 0:1], in1=xt_sb[:, 1, halves, cols],
                                               op0=ALU.mult, op1=ALU.add).then_inc(last_z_made, 1)

            def last_norm(n):
                r = (n - (CHUNKS - 1)) * 2
                dve.wait_ge(shift_made, n + 1)
                dve.wait_ge(stored, (CHUNKS - 1) * 16)
                nc.vector.tensor_scalar(normed[:, r * C:(r + 1) * C], summed[:, r, :], rstd[:, r:r + 1],
                                        shift[:, r:r + 1], ALU.mult, ALU.add).then_inc(last_norm_made, 1)

            dve.wait_ge(xt_scaled, CHUNKS)
            last_z(ROWS_A, slice(0, HALVES), 1, 1)
            nc.vector.scalar_tensor_tensor(out=xt_sb[:, 1, :, ROWS_B], in0=y_ps[1][:, :, ROWS_B],
                                           scalar=t_col[:, 0:1], in1=xt_sb[:, 1, :, ROWS_B], op0=ALU.mult,
                                           op1=ALU.add).then_inc(xt_scaled, 1)
            sums(CHUNKS - 1, slice(0, 2))
            dve.wait_ge(xt_scaled, CHUNKS + 1)
            last_z(ROWS_B, slice(0, 1), 0, 2)
            scale_and_shift(CHUNKS - 1, CHUNKS - 1, slice(0, 2))
            last_norm(CHUNKS - 1)
            last_z(ROWS_B, slice(1, 2), 0, 3)
            sums(CHUNKS - 1, slice(2, 4))
            scale_and_shift(CHUNKS - 1, CHUNKS, slice(2, 4))
            last_norm(CHUNKS)

        @block.tensor
        def _(pe):
            pe.wait_ge(idle_made, 1)
            for _ in range(WARM):
                nc.tensor.matmul(proj_ps[0][:, :], idle[:, 0:P], idle[:, :], start=True, stop=True)

            def project(q):
                pe.wait_ge(z_hi_made, (q + 1) * HALVES)
                pe.wait_ge(z_lo_made, (q + 1) * HALVES)
                for r in range(ROW_TILES):
                    rows = slice(r * P, (r + 1) * P)
                    for h in range(HALVES):
                        feats = slice(h * C, (h + 1) * C)
                        for i, (zp, wp) in enumerate([(z_hi, w_hi), (z_hi, w_lo), (z_lo, w_hi)]):
                            last = nc.tensor.matmul(proj_ps[r][:, 0:C], zp[:, h, rows], wp[:, feats],
                                                    start=(h == 0 and i == 0), stop=(h == HALVES - 1 and i == 2))
                    last.then_inc(projected, 1)

            def part_by_part(k, tiles, made):
                x_hi_ready, adj_hi_ready, x_lo_ready, adj_lo_ready = made
                for waits, xp, ap in [((x_hi_ready, adj_hi_ready), x_hi, adj_hi), ((x_lo_ready,), x_lo, adj_hi),
                                      ((adj_lo_ready,), x_hi, adj_lo)]:
                    for ready, count in waits:
                        pe.wait_ge(ready, count)
                    for tile in tiles:
                        cols = slice((tile - k * PIECE) * COLS, (tile - k * PIECE + 1) * COLS)
                        for h in range(HALVES):
                            last = nc.tensor.matmul(y_ps[0][:, h, :], xp[:, tile, h * P:(h + 1) * P],
                                                    ap[:, k % PARTS, cols],
                                                    start=(tile == 0 and xp is x_hi and ap is adj_hi),
                                                    stop=(tile == TILES - 1 and ap is adj_lo))
                return last

            def tile_half(b, k, j, h, rows=slice(0, COLS), first_tile=0, last_tile=TILES - 1):
                tile = k * PIECE + j
                cols = slice(j * COLS + rows.start, j * COLS + rows.stop)
                feats = slice(h * P, (h + 1) * P)
                for i, (xp, ap) in enumerate([(x_hi, adj_hi), (x_hi, adj_lo), (x_lo, adj_hi)]):
                    last = nc.tensor.matmul(y_ps[b][:, h, rows], xp[:, tile, feats], ap[:, k % PARTS, cols],
                                            start=(tile == first_tile and i == 0),
                                            stop=(tile == last_tile and i == 2))
                return last

            def aggregate(q, b):
                for k in range(PIECES - PARTS if static(q) and q == CHUNKS - 1 else PIECES):
                    if static(q) and q == 0:
                        if k == 0:
                            part_by_part(0, [0], [(first_x_hi_made, 1), (first_adj_hi_made, 1),
                                                  (first_x_lo_made, 1), (first_adj_lo_made, 1)])
                        last = part_by_part(k, range(max(1, k * PIECE), (k + 1) * PIECE),
                                            [(x_hi_made, k + 1), (adj_hi_made, k + 1),
                                             (x_lo_made, k + 1), (adj_lo_made, k + 1)])
                    else:
                        pe.wait_ge(adj_lo_made, q * PIECES + (k + 1))
                        for j in range(PIECE):
                            for h in range(HALVES):
                                last = tile_half(b, k, j, h)
                    last.then_inc(adj_used, 1)
                    if k == PROJECT_AT and (not static(q) or q > 0):
                        project(q - 1)

            chunks(pe, aggregate)

            last_tiles = [(k, j) for k in range(PIECES - PARTS, PIECES) for j in range(PIECE)]

            def project_last(rows, h, z_parts):
                pe.wait_ge(last_z_made, z_parts)
                for r in rows:
                    last = nc.tensor.matmul(proj_ps[r][:, 0:C], z[:, h, r * P:(r + 1) * P],
                                            w_raw[:, h * C:(h + 1) * C], start=(h == 0), stop=(h == HALVES - 1))
                    if h == HALVES - 1:
                        last.then_inc(projected, 1)

            for k, j in last_tiles:
                if j == 0:
                    pe.wait_ge(adj_lo_made, (CHUNKS - 1) * PIECES + k + 1)
                for h in range(HALVES):
                    last = tile_half(1, k, j, h, ROWS_A)
            last.then_inc(last_y_made, 1)
            pe.wait_ge(z_made, (CHUNKS - 1) * HALVES)
            for h in range(HALVES):
                for n, (k, j) in enumerate(last_tiles):
                    last = tile_half(0, k, j, h, ROWS_B, first_tile=TILES - len(last_tiles))
                    if n == len(last_tiles) // 2 - 1:
                        if h == 0:
                            pe.wait_ge(sum_made, (CHUNKS - 1) * ROW_TILES)
                            project_last([0, 1], 0, 1)
                            project_last([0, 1], 1, 1)
                        else:
                            project_last([2, 3], 0, 2)
                last.then_inc(last_y_made, 1)
            project_last([2, 3], 1, 3)


def kernel(x, adj, L0_gnn_t, L0_gnn_weight):
    import numpy as _np
    import concourse.bacc as _bacc
    from concourse import mybir as _mybir
    from concourse.bass_utils import run_bass_kernel_spmd as _run

    x, adj = _np.asarray(x), _np.asarray(adj)
    arrays = {
        "x_rows": x.reshape(P, TILES * C),
        "x_cols": x.reshape(P, CHUNKS, ROW_TILES, HALVES, P).transpose(1, 4, 3, 2, 0)
                   .reshape(CHUNKS, P, HALVES, COLS),
        "adj_cols": adj.reshape(P, CHUNKS, ROW_TILES, P, PIECES, PIECE).transpose(1, 4, 3, 5, 2, 0)
                       .reshape(CHUNKS, PIECES, P, PIECE * COLS),
        "t": _np.asarray(L0_gnn_t),
        "weight": _np.asarray(L0_gnn_weight),
    }
    arrays = {name: _np.ascontiguousarray(a) for name, a in arrays.items()}
    nc = _bacc.Bacc("TRN2", target_bir_lowering=False, num_devices=1)
    args = [nc.dram_tensor(name, a.shape, _mybir.dt.from_np(a.dtype), kind="ExternalInput").ap()
            for name, a in arrays.items()]
    args.append(nc.dram_tensor("out", (N, C), F32, kind="ExternalOutput").ap())
    gnn_resnorm(nc, *args)
    r = _run(nc, [arrays], core_ids=[0])
    return r.results[0]["out"]
```
